# Optimizing a Trainium2 kernel written in Bass

```python
import numpy as np
import jax
import jax.numpy as jnp

def _softmax(x, axis=-1):
    return jax.nn.softmax(x, axis=axis)

def _gelu(x):
    return jax.nn.gelu(x, approximate=True)

def _silu(x):
    return jax.nn.silu(x)

def _sigmoid(x):
    return jax.nn.sigmoid(x)

def _layernorm(x, axis=-1, eps=1e-05):
    m = jnp.mean(x, axis=axis, keepdims=True)
    v = jnp.var(x, axis=axis, keepdims=True)
    return (x - m) / jnp.sqrt(v + eps)

def _scatter_add(tgt, idx, src, axis=0):
    return tgt.at[idx].add(src)

def _segment_sum(src, seg, n):
    return jax.ops.segment_sum(src, seg, n)
kernel_name = 'mk_conv_seq_d2_conv_nchw256_r2_e12889'

def setup_inputs(seed: int=0):
    np.random.seed(seed)
    _w = jnp.asarray

    def _rec_inputs():
        import jax
        import jax.numpy as jnp
        _gk = jax.random.key(seed)
        x = -0.0002928 + 1 * jax.random.normal(jax.random.fold_in(_gk, 1), (4, 128, 32, 32), jnp.float32)
        return x
    x = _rec_inputs()

    def _L0_conv_setup():
        import jax, jax.numpy as jnp
        import numpy as np
        B, C, H, W = (4, 128, 32, 32)
        RD = C // 8
        key = jax.random.key(seed)
        ks = jax.random.split(key, 7)
        s = 0.05
        return {'x': jax.random.normal(ks[0], (B, C, H, W), dtype=jnp.float32), 'Wq': jax.random.normal(ks[1], (RD, C), dtype=jnp.float32) * s, 'bq': jax.random.normal(ks[2], (RD,), dtype=jnp.float32) * s, 'Wk': jax.random.normal(ks[3], (RD, C), dtype=jnp.float32) * s, 'bk': jax.random.normal(ks[4], (RD,), dtype=jnp.float32) * s, 'Wv': jax.random.normal(ks[5], (C, C), dtype=jnp.float32) * s, 'bv': jax.random.normal(ks[6], (C,), dtype=jnp.float32) * s, 'gamma': jnp.ones((1,), dtype=jnp.float32) * 0.5}
    _L0_conv_all = _L0_conv_setup()
    _L0_conv_in = {k: v for k, v in _L0_conv_all.items() if k in ('Wq', 'bq', 'Wk', 'bk', 'Wv', 'bv', 'gamma')}
    del _L0_conv_all

    def _L1_conv_setup():
        import jax, jax.numpy as jnp
        import numpy as np
        C = 128
        CQK = C // 8
        key = jax.random.key(seed)
        ks = jax.random.split(key, 8)
        x = jax.random.normal(ks[0], (4, C, 32, 32), dtype=jnp.float32)
        wq = jax.random.normal(ks[1], (CQK, C), dtype=jnp.float32) * (1.0 / np.sqrt(C))
        bq = jnp.zeros((CQK,), dtype=jnp.float32)
        wk = jax.random.normal(ks[2], (CQK, C), dtype=jnp.float32) * (1.0 / np.sqrt(C))
        bk = jnp.zeros((CQK,), dtype=jnp.float32)
        wv = jax.random.normal(ks[3], (C, C), dtype=jnp.float32) * (1.0 / np.sqrt(C))
        bv = jnp.zeros((C,), dtype=jnp.float32)
        gamma = jax.random.normal(ks[4], (1,), dtype=jnp.float32) * 0.1
        return {'x': x, 'wq': wq, 'bq': bq, 'wk': wk, 'bk': bk, 'wv': wv, 'bv': bv, 'gamma': gamma}
    _L1_conv_all = _L1_conv_setup()
    _L1_conv_in = {k: v for k, v in _L1_conv_all.items() if k in ('wq', 'bq', 'wk', 'bk', 'wv', 'bv', 'gamma')}
    del _L1_conv_all
    return {'x': x, 'L0_conv_Wq': _L0_conv_in['Wq'], 'L0_conv_bq': _L0_conv_in['bq'], 'L0_conv_Wk': _L0_conv_in['Wk'], 'L0_conv_bk': _L0_conv_in['bk'], 'L0_conv_Wv': _L0_conv_in['Wv'], 'L0_conv_bv': _L0_conv_in['bv'], 'L0_conv_gamma': _L0_conv_in['gamma'], 'L1_conv_wq': _L1_conv_in['wq'], 'L1_conv_bq': _L1_conv_in['bq'], 'L1_conv_wk': _L1_conv_in['wk'], 'L1_conv_bk': _L1_conv_in['bk'], 'L1_conv_wv': _L1_conv_in['wv'], 'L1_conv_bv': _L1_conv_in['bv'], 'L1_conv_gamma': _L1_conv_in['gamma']}

def reference(x, L0_conv_Wq, L0_conv_bq, L0_conv_Wk, L0_conv_bk, L0_conv_Wv, L0_conv_bv, L0_conv_gamma, L1_conv_wq, L1_conv_bq, L1_conv_wk, L1_conv_bk, L1_conv_wv, L1_conv_bv, L1_conv_gamma):
    import jax
    import jax.numpy as jnp

    def _L0_conv_ref(x, Wq, bq, Wk, bk, Wv, bv, gamma):
        import jax, jax.numpy as jnp
        import numpy as np
        B, C, H, W = (4, 128, 32, 32)
        RD = C // 8
        b, c, h, w = x.shape
        n = h * w
        xf = x.reshape(b, c, n)
        q = jnp.einsum('rc,bcn->brn', Wq, xf) + bq[None, :, None]
        k = jnp.einsum('rc,bcn->brn', Wk, xf) + bk[None, :, None]
        v = jnp.einsum('oc,bcn->bon', Wv, xf) + bv[None, :, None]
        energy = jnp.einsum('bri,brj->bij', q, k)
        attn = jax.nn.softmax(energy, axis=2)
        out = jnp.einsum('bcj,bij->bci', v, attn).reshape(b, c, h, w)
        return gamma * out + x

    def _L1_conv_ref(x, wq, bq, wk, bk, wv, bv, gamma):
        import jax, jax.numpy as jnp
        import numpy as np
        C = 128
        CQK = C // 8
        B, Cc, H, W = x.shape
        N = H * W
        xf = x.reshape(B, Cc, N)
        q = jnp.einsum('oc,bcn->bno', wq, xf) + bq
        k = jnp.einsum('oc,bcn->bon', wk, xf) + bk[None, :, None]
        attn = jax.nn.softmax(jnp.einsum('bnd,bdm->bnm', q, k), axis=-1)
        v = jnp.einsum('oc,bcn->bon', wv, xf) + bv[None, :, None]
        out = jnp.einsum('bcn,bmn->bcm', v, attn).reshape(B, Cc, H, W)
        return gamma[0] * out + x

    def _gn(v, G=32, eps=1e-05):
        B_, C_, H_, W_ = v.shape
        g = v.reshape(B_, G, C_ // G, H_, W_)
        m = jnp.mean(g, axis=(2, 3, 4), keepdims=True)
        s = jnp.var(g, axis=(2, 3, 4), keepdims=True)
        return ((g - m) / jnp.sqrt(s + eps)).reshape(v.shape)

    def _ln_c(v, eps=1e-06):
        m = jnp.mean(v, axis=1, keepdims=True)
        s = jnp.var(v, axis=1, keepdims=True)
        return (v - m) / jnp.sqrt(s + eps)

    def _ln_t(v, eps=1e-05):
        m = jnp.mean(v, axis=-1, keepdims=True)
        s = jnp.var(v, axis=-1, keepdims=True)
        return (v - m) / jnp.sqrt(s + eps)

    def _to_tokens(v):
        B_, C_, H_, W_ = v.shape
        return v.reshape(B_, C_, H_ * W_).transpose(0, 2, 1)

    def _from_tokens(t, like):
        B_, C_, H_, W_ = like.shape
        return t.transpose(0, 2, 1).reshape(B_, C_, H_, W_)
    x = _L0_conv_ref(x, L0_conv_Wq, L0_conv_bq, L0_conv_Wk, L0_conv_bk, L0_conv_Wv, L0_conv_bv, L0_conv_gamma)
    x = _L1_conv_ref(x, L1_conv_wq, L1_conv_bq, L1_conv_wk, L1_conv_bk, L1_conv_wv, L1_conv_bv, L1_conv_gamma)
    return x

_drawn_inputs = setup_inputs


def setup_inputs(seed=0):
    import zlib

    import numpy as np

    out = dict(_drawn_inputs(seed))
    spreads = {'L1_conv_bq': (0.0, 0.8), 'L1_conv_bk': (0.0, 0.8), 'L1_conv_bv': (0.0, 0.7)}
    factors = {'L0_conv_bq': 8.0, 'L0_conv_bk': 8.0}
    for name, (base, spread) in spreads.items():
        noise = np.random.default_rng([zlib.crc32(name.encode()), seed]).standard_normal(out[name].shape)
        drawn = base * np.exp(spread * noise) if base else spread * noise
        out[name] = jnp.asarray(drawn.astype(out[name].dtype))
    for name, factor in factors.items():
        out[name] = (out[name] * factor).astype(out[name].dtype)
    return out
```

```python
from contextlib import ExitStack

import concourse.bass as bass
from concourse import mybir

B, C, N, RD = 4, 128, 1024, 16
LAYERS = 2
STAGES = LAYERS * B
P = 128
TILES = N // P
HALF = N // 2
SHIFT_ROW = 3 * RD
NATIVE = 4
ORDER = [0, 4, 1, 5, 2, 6, 3, 7]
CUT = TILES - NATIVE
LEAD = 2


def build_attention_layers(nc, x_in, wqk_in, wv_in, columns_in, bv_in, identity_in, out):
    fp32 = mybir.dt.float32
    fp32r = mybir.dt.float32r
    ALU = mybir.AluOpType
    ACT = mybir.ActivationFunctionType
    AX = mybir.AxisListType

    ctx = ExitStack()
    with ctx:
        def sb(name, shape, dt=fp32):
            return ctx.enter_context(nc.sbuf_tensor(name, shape, dt))

        def sem(name):
            return ctx.enter_context(nc.semaphore(name))

        x_all = sb("x_all", [P, STAGES + B, N])
        wqk = sb("wqk", [P, LAYERS, P])
        wv = sb("wv", [P, LAYERS, C])
        columns = sb("columns", [P, 2 * LAYERS + 1])
        bv_rows = sb("bv_rows", [P, LAYERS, C])
        identity = sb("identity", [P, P])
        wqk_hi = sb("wqk_hi", [P, LAYERS, P], fp32r)
        wqk_lo = sb("wqk_lo", [P, LAYERS, P], fp32r)
        wv_hi = sb("wv_hi", [P, LAYERS, C], fp32r)
        wv_lo = sb("wv_lo", [P, LAYERS, C], fp32r)
        x_hi = [sb(f"x_hi{p}", [P, N], fp32r) for p in range(2)]
        x_lo = [sb(f"x_lo{p}", [P, N], fp32r) for p in range(2)]
        masked_hi = sb("masked_hi", [P, N], fp32r)
        qk = [sb(f"qk{p}", [P, N], fp32r) for p in range(2)]
        qk_swapped = [sb(f"qk_swapped{p}", [P, N], fp32r) for p in range(2)]
        q_shifted = [sb(f"q_shifted{p}", [P, N], fp32r) for p in range(2)]
        k_twice = [sb(f"k_twice{p}", [P, N], fp32r) for p in range(2)]
        neg_max = [sb(f"neg_max{p}", [P, TILES]) for p in range(2)]
        row_sum = [sb(f"row_sum{p}", [P, TILES]) for p in range(2)]
        log_sum = [sb(f"log_sum{p}", [P, TILES]) for p in range(2)]
        shift = [sb(f"shift{p}", [P, TILES]) for p in range(2)]
        shift_rows = sb("shift_rows", [TILES, 2, P], fp32r)
        v32 = [sb(f"v32_{p}", [P, TILES, C]) for p in range(2)]
        v_hi = [sb(f"v_hi{p}", [P, CUT, C], fp32r) for p in range(2)]
        v_lo = [sb(f"v_lo{p}", [P, CUT, C], fp32r) for p in range(2)]
        attn = sb("attn", [P, TILES, N])
        attn_hi = sb("attn_hi", [P, CUT, N], fp32r)
        attn_lo = sb("attn_lo", [P, CUT, N], fp32r)

        e_ring = [ctx.enter_context(nc.psum_tensor(f"e_ring{i}", [P, N], fp32)) for i in range(2)]
        et_psum = ctx.enter_context(nc.psum_tensor("et_psum", [P, N], fp32))
        out_psum = ctx.enter_context(nc.psum_tensor("out_psum", [P, N], fp32))

        x_loaded = [sem(f"x_loaded{b}") for b in range(B)]
        wqk_loaded, wv_loaded, small_loaded = sem("wqk_loaded"), sem("wv_loaded"), sem("small_loaded")
        wqk_hi_made, wqk_cut, wv_hi_made, wv_cut = sem("wqk_hi_made"), sem("wqk_cut"), sem("wv_hi_made"), sem("wv_cut")
        x0_hi_made, x0_cut = sem("x0_hi_made"), sem("x0_cut")
        x_hi_made, x_cut = sem("x_hi_made"), sem("x_cut")
        qk_mm, masked_made, qk_made = sem("qk_mm"), sem("masked_made"), sem("qk_made")
        swapped, twice = sem("swapped"), sem("twice")
        v_mm, v32_made, v_hi_made, v_made = sem("v_mm"), sem("v32_made"), sem("v_hi_made"), sem("v_made")
        e_mm, max_made, sum_made = sem("e_mm"), sem("max_made"), sem("sum_made")
        log_made, shift_made, shift_mm = sem("log_made"), sem("shift_made"), sem("shift_mm")
        shift_hi_made, shift_cut, shift_placed = sem("shift_hi_made"), sem("shift_cut"), sem("shift_placed")
        et_mm, attn_made = sem("et_mm"), sem("attn_made")
        attn_hi_made, attn_cut = sem("attn_hi_made"), sem("attn_cut")
        pv_mm, x_made, stored = sem("pv_mm"), sem("x_made"), sem("stored")

        block = ctx.enter_context(nc.Block())

        def at_least(engine, semaphore, value):
            if value > 0:
                engine.wait_ge(semaphore, value)

        def layer(s):
            return s // B

        def cut_before(k):
            return sum(j >= NATIVE for j in ORDER[:k])

        def e_tile(s, k):
            stage, i = (s + 1, k + 4) if k < 4 else (s + 2, k - 4)
            return (stage, i) if 0 <= stage < STAGES else None

        def et_tile(s, k):
            stage, i = (s, k + LEAD) if k + LEAD < TILES else (s + 1, k + LEAD - TILES)
            return (stage, i) if 0 <= stage < STAGES else None

        def e_slot(stage, i):
            turn = {4: 0, 5: 1, 6: 3, 7: 5, 0: 7, 1: 8, 2: 9, 3: 10}[i]
            step = stage - 1 if i >= 4 else stage - 2
            return (step + turn) % 2

        def qk_slot(stage):
            return (stage - 2 + 2) % 2

        def v_slot(stage):
            return (stage - 1 + 4) % 2

        def shift_slot(stage):
            return (stage - 1 + 6) % 2

        @block.sync
        def _(sp):
            sp.dma_start(x_all[:, 0], x_in[0]).then_inc(x_loaded[0], 16)
            sp.dma_start(x_all[:, 1], x_in[1]).then_inc(x_loaded[1], 16)
            sp.dma_start(x_all[:, 2], x_in[2]).then_inc(x_loaded[2], 16)
            sp.dma_start(x_all[:, 3], x_in[3]).then_inc(x_loaded[3], 16)

            def swap_qk(s):
                sp.wait_ge(qk_made, s + 1)
                a, b = qk[s % 2][:].bitcast(fp32), qk_swapped[s % 2][:].bitcast(fp32)
                sp.dma_start(b[64:128, :], a[0:64, :]).then_inc(swapped, 16)
                sp.dma_start(b[0:64, :], a[64:128, :]).then_inc(swapped, 16)

            def copy_qk(s):
                sp.wait_ge(qk_made, s + 1)
                at_least(sp, et_mm, TILES * (s - 1))
                a, q2, k2 = (t[s % 2][:].bitcast(fp32) for t in (qk, q_shifted, k_twice))
                for half in (0, 64):
                    sp.dma_start(q2[half:half + 64, :], a[0:64, :]).then_inc(twice, 16)
                    sp.dma_start(k2[half:half + 64, :], a[64:128, :]).then_inc(twice, 16)

            def place_shift(s):
                sp.wait_ge(shift_cut, s + 1)
                sp.wait_ge(twice, 64 * (s + 1))
                for half in (0, 64):
                    for part in range(2):
                        row = half + SHIFT_ROW + part
                        to = q_shifted[s % 2][row:row + 1, :].bitcast(fp32).rearrange("p (i n) -> p i n", n=P)
                        sp.dma_start(to, shift_rows[:, part, :].bitcast(fp32)).then_inc(shift_placed, 16)

            def store(s):
                sp.wait_ge(x_made, 2 * (s + 1))
                sp.dma_start(out[s - B], x_all[:, s + B]).then_inc(stored, 16)

            for s in range(-2, STAGES):
                if 0 <= s + 1 < STAGES:
                    copy_qk(s + 1)
                if s + 2 < STAGES:
                    swap_qk(s + 2)
                if s - 1 >= B:
                    store(s - 1)
                if 0 <= s + 1 < STAGES:
                    place_shift(s + 1)
            store(STAGES - 1)
            sp.wait_ge(stored, 16 * B)

        @block.gpsimd
        def _(pool):
            def cut_x(s):
                p = s % 2
                if s < B:
                    pool.wait_ge(x_loaded[s], 16)
                else:
                    pool.wait_ge(x_made, 2 * (s - B + 1))
                at_least(pool, v_mm, s - 1)
                at_least(pool, qk_mm, s - 1)
                nc.gpsimd.tensor_scalar(x_hi[p][:], x_all[:, s], 1.0, 0.0, ALU.mult,
                                        ALU.add).then_inc(x_hi_made, 1)
                pool.wait_ge(x_hi_made, s)
                nc.gpsimd.tensor_tensor(x_lo[p][:], x_all[:, s], x_hi[p][:].bitcast(fp32),
                                        ALU.subtract).then_inc(x_cut, 1)

            def cut_attn(s, k):
                j = ORDER[k]
                if j < NATIVE:
                    return
                pool.wait_ge(attn_made, TILES * s + k + 1)
                at_least(pool, pv_mm, TILES * (s - 1) + k + 1)
                nc.gpsimd.tensor_scalar(attn_hi[:, j - NATIVE], attn[:, j], 1.0, 0.0, ALU.mult,
                                        ALU.add).then_inc(attn_hi_made, 1)
                pool.wait_ge(attn_hi_made, CUT * s + cut_before(k) + 1)
                nc.gpsimd.tensor_tensor(attn_lo[:, j - NATIVE], attn[:, j],
                                        attn_hi[:, j - NATIVE].bitcast(fp32),
                                        ALU.subtract).then_inc(attn_cut, 1)

            for s in range(-2, STAGES):
                for k in range(TILES):
                    if et_tile(s, k):
                        cut_attn(*et_tile(s, k))
                    if k == 3 and s + 3 < STAGES:
                        cut_x(s + 3)

        @block.scalar
        def _(act):
            act.preload_act_table_set("natural_log_exp_and_others")
            act.dma_start(wqk[:], wqk_in).then_inc(wqk_loaded, 16)
            act.dma_start(columns[:], columns_in).then_inc(small_loaded, 16)
            act.dma_start(identity[:], identity_in).then_inc(small_loaded, 16)
            act.dma_start(bv_rows[:], bv_in).then_inc(small_loaded, 16)
            act.dma_start(wv[:], wv_in).then_inc(wv_loaded, 16)

            def row_sums(s, i):
                act.wait_ge(max_made, TILES * s + i + 1)
                e = e_ring[e_slot(s, i)]
                nc.scalar.activation(e[:], e[:], ACT.Exp, bias=neg_max[s % 2][:, i:i + 1],
                                     accum_out=row_sum[s % 2][:, i:i + 1]).then_inc(sum_made, 1)

            def log_sums(s):
                act.wait_ge(sum_made, TILES * (s + 1))
                nc.scalar.activation(log_sum[s % 2][:], row_sum[s % 2][:], ACT.Ln).then_inc(log_made, 1)

            def attention(s, k):
                j = ORDER[k]
                act.wait_ge(et_mm, TILES * s + k + 1)
                if j < NATIVE:
                    at_least(act, pv_mm, TILES * (s - 1) + k + 1)
                elif s > 0:
                    act.wait_ge(attn_cut, CUT * (s - 1) + cut_before(k) + 1)
                nc.scalar.activation(attn[:, j], et_psum[:], ACT.Exp).then_inc(attn_made, 1)

            for s in range(-2, STAGES):
                for k in range(TILES):
                    if et_tile(s, k):
                        attention(*et_tile(s, k))
                    if e_tile(s, k):
                        row_sums(*e_tile(s, k))
                    if k == 3 and 0 <= s + 1 < STAGES:
                        log_sums(s + 1)

        @block.vector
        def _(dve):
            dve.wait_ge(wqk_loaded, 16)
            nc.vector.tensor_copy(wqk_hi[:], wqk[:]).then_inc(wqk_hi_made, 1)
            dve.wait_ge(wqk_hi_made, 1)
            nc.vector.tensor_tensor(wqk_lo[:], wqk[:], wqk_hi[:].bitcast(fp32),
                                    ALU.subtract).then_inc(wqk_cut, 1)
            dve.wait_ge(x_loaded[0], 16)
            nc.vector.tensor_copy(x_hi[0][:], x_all[:, 0]).then_inc(x0_hi_made, 1)
            dve.wait_ge(x0_hi_made, 1)
            nc.vector.tensor_tensor(x_lo[0][:], x_all[:, 0], x_hi[0][:].bitcast(fp32),
                                    ALU.subtract).then_inc(x0_cut, 1)
            dve.wait_ge(small_loaded, 48)

            def stack_qk(s):
                src, bias = e_ring[qk_slot(s)], columns[:, layer(s):layer(s) + 1]
                mask = columns[:, 2 * LAYERS:2 * LAYERS + 1]
                dve.wait_ge(qk_mm, s + 1)
                at_least(dve, qk_made, s)
                nc.vector.tensor_scalar(masked_hi[:], src[:], bias, mask, ALU.add,
                                        ALU.mult).then_inc(masked_made, 1)
                dve.wait_ge(masked_made, s + 1)
                at_least(dve, e_mm, TILES * (s - 1))
                at_least(dve, swapped, 32 * (s - 1))
                at_least(dve, twice, 64 * (s - 1))
                nc.vector.scalar_tensor_tensor(out=qk[s % 2][:], in0=src[:], scalar=bias,
                                               in1=masked_hi[:].bitcast(fp32), op0=ALU.add,
                                               op1=ALU.subtract).then_inc(qk_made, 1)

            def make_v(s):
                p, src = s % 2, e_ring[v_slot(s)][:].rearrange("p (j c) -> p j c", c=C)
                bias = bv_rows[:, layer(s)][:, None, :].to_broadcast([P, TILES, C])
                dve.wait_ge(v_mm, s + 1)
                at_least(dve, pv_mm, TILES * (s - 1))
                nc.vector.tensor_tensor(v32[p][:], src, bias, ALU.add).then_inc(v32_made, 1)
                dve.wait_ge(v32_made, s + 1)
                nc.vector.tensor_copy(v_hi[p][:], v32[p][:, NATIVE:]).then_inc(v_hi_made, 1)
                dve.wait_ge(v_hi_made, s + 1)
                nc.vector.tensor_tensor(v_lo[p][:], v32[p][:, NATIVE:], v_hi[p][:].bitcast(fp32),
                                        ALU.subtract).then_inc(v_made, 1)

            def row_max(s, i):
                dve.wait_ge(e_mm, TILES * s + i + 1)
                nc.vector.tensor_reduce(neg_max[s % 2][:, i:i + 1], e_ring[e_slot(s, i)][:], axis=AX.X,
                                        op=ALU.max, negate=True).then_inc(max_made, 1)

            def make_shift(s):
                dve.wait_ge(log_made, s + 1)
                dve.wait_ge(max_made, TILES * (s + 1))
                nc.vector.scalar_tensor_tensor(out=shift[s % 2][:], in0=log_sum[s % 2][:], scalar=-1.0,
                                               in1=neg_max[s % 2][:], op0=ALU.mult,
                                               op1=ALU.add).then_inc(shift_made, 1)

            def cut_shift(s):
                rows = e_ring[shift_slot(s)][0:TILES, 0:P]
                dve.wait_ge(shift_mm, s + 1)
                at_least(dve, shift_placed, 64 * s)
                nc.vector.tensor_copy(shift_rows[:, 0, :], rows).then_inc(shift_hi_made, 1)
                dve.wait_ge(shift_hi_made, s + 1)
                nc.vector.tensor_tensor(shift_rows[:, 1, :], rows, shift_rows[:, 0, :].bitcast(fp32),
                                        ALU.subtract).then_inc(shift_cut, 1)

            def finish(s):
                dve.wait_ge(pv_mm, TILES * (s + 1))
                gamma = columns[:, LAYERS + layer(s):LAYERS + layer(s) + 1]
                for h in range(2):
                    part = slice(h * HALF, (h + 1) * HALF)
                    nc.vector.scalar_tensor_tensor(out=x_all[:, s + B, part], in0=out_psum[:, part],
                                                   scalar=gamma, in1=x_all[:, s, part], op0=ALU.mult,
                                                   op1=ALU.add).then_inc(x_made, 1)

            for s in range(-2, STAGES):
                if s - 1 >= 0:
                    finish(s - 1)
                for k in range(TILES):
                    if e_tile(s, k):
                        row_max(*e_tile(s, k))
                    if k == 1 and s + 2 < STAGES:
                        stack_qk(s + 2)
                    if k == 2 and 0 <= s + 1 < STAGES:
                        make_v(s + 1)
                    if k == 4 and 0 <= s + 1 < STAGES:
                        make_shift(s + 1)
                        cut_shift(s + 1)
                if s == -2:
                    dve.wait_ge(wv_loaded, 16)
                    nc.vector.tensor_copy(wv_hi[:], wv[:]).then_inc(wv_hi_made, 1)
                    dve.wait_ge(wv_hi_made, 1)
                    nc.vector.tensor_tensor(wv_lo[:], wv[:], wv_hi[:].bitcast(fp32),
                                            ALU.subtract).then_inc(wv_cut, 1)
            finish(STAGES - 1)

        @block.tensor
        def _(pe):
            def project_qk(s):
                p, l, to = s % 2, layer(s), e_ring[qk_slot(s)]
                if s == 0:
                    pe.wait_ge(wqk_cut, 1)
                    pe.wait_ge(x0_cut, 1)
                else:
                    pe.wait_ge(x_cut, s)
                at_least(pe, sum_made, TILES * (s - 1) + 5)
                for n, (w, x) in enumerate(((wqk_hi, x_hi[p]), (wqk_hi, x_lo[p]), (wqk_lo, x_hi[p]))):
                    for h in range(2):
                        part = slice(h * HALF, (h + 1) * HALF)
                        last = nc.tensor.matmul(to[:, part], w[:, l, :], x[:, part], start=(n == 0),
                                                stop=(n == 2))
                last.then_inc(qk_mm, 1)

            def project_v(s):
                p, l, to = s % 2, layer(s), e_ring[v_slot(s)]
                if s == 0:
                    pe.wait_ge(wv_cut, 1)
                if s + 1 < STAGES:
                    pe.wait_ge(qk_made, s + 2)
                else:
                    pe.wait_ge(sum_made, TILES * s + 5)
                for j in range(TILES):
                    part = slice(j * P, (j + 1) * P)
                    for n, (x, w) in enumerate(((x_hi[p], wv_hi), (x_hi[p], wv_lo), (x_lo[p], wv_hi))):
                        last = nc.tensor.matmul(to[:, j * C:(j + 1) * C], x[:, part], w[:, l, :],
                                                start=(n == 0), stop=(n == 2))
                last.then_inc(v_mm, 1)

            def energies(s, i):
                p, to, rows = s % 2, e_ring[e_slot(s, i)], slice(i * P, (i + 1) * P)
                if i == 0:
                    pe.wait_ge(swapped, 32 * (s + 1))
                if i == 1:
                    at_least(pe, shift_cut, s)
                else:
                    at_least(pe, sum_made, TILES * s + {0: 0, 2: 1, 3: 2, 4: 3, 5: 4, 6: 6, 7: 7}[i])
                if i == 1:
                    at_least(pe, v_made, s)
                nc.tensor.matmul(to[:, 0:HALF], qk[p][0:64, rows], qk_swapped[p][0:64, 0:HALF],
                                 start=True, stop=True)
                nc.tensor.matmul(to[:, HALF:N], qk_swapped[p][64:128, rows], qk[p][64:128, HALF:N],
                                 start=True, stop=True).then_inc(e_mm, 1)

            def transpose_shift(s):
                if s == 0:
                    pe.wait_ge(small_loaded, 48)
                pe.wait_ge(v_made, s + 1)
                pe.wait_ge(shift_made, s + 1)
                nc.tensor.transpose(e_ring[shift_slot(s)][0:TILES, 0:P], shift[s % 2][:],
                                    identity[:]).then_inc(shift_mm, 1)

            def energies_transposed(s, k):
                p, j = s % 2, ORDER[k]
                rows = slice(j * P, (j + 1) * P)
                if k == 0:
                    pe.wait_ge(shift_placed, 64 * (s + 1))
                at_least(pe, attn_made, TILES * s + k)
                nc.tensor.matmul(et_psum[:, 0:HALF], k_twice[p][0:64, rows], q_shifted[p][0:64, 0:HALF],
                                 start=True, stop=True)
                nc.tensor.matmul(et_psum[:, HALF:N], k_twice[p][64:128, rows],
                                 q_shifted[p][64:128, HALF:N], start=True, stop=True).then_inc(et_mm, 1)

            def times_v(s, k):
                p, j = s % 2, ORDER[k]
                if k == 0:
                    pe.wait_ge(v_made, s + 1)
                if j < NATIVE:
                    pe.wait_ge(attn_made, TILES * s + k + 1)
                    passes = ((v32[p][:, j], attn[:, j]),)
                else:
                    pe.wait_ge(attn_cut, CUT * s + cut_before(k) + 1)
                    c = j - NATIVE
                    passes = ((v_hi[p][:, c], attn_hi[:, c]), (v_hi[p][:, c], attn_lo[:, c]),
                              (v_lo[p][:, c], attn_hi[:, c]))
                for n, (v, a) in enumerate(passes):
                    for h in range(2):
                        part = slice(h * HALF, (h + 1) * HALF)
                        if k == 0 and n == 0:
                            at_least(pe, x_made, 2 * (s - 1) + h + 1)
                        last = nc.tensor.matmul(out_psum[:, part], v, a[:, part],
                                                start=(k == 0 and n == 0),
                                                stop=(k == TILES - 1 and n == len(passes) - 1))
                last.then_inc(pv_mm, 1)

            for s in range(-2, STAGES):
                for k in range(TILES):
                    if et_tile(s, k):
                        energies_transposed(*et_tile(s, k))
                    if e_tile(s, k):
                        energies(*e_tile(s, k))
                    if k == 1 and s + 2 < STAGES:
                        project_qk(s + 2)
                    if k == 2 and 0 <= s + 1 < STAGES:
                        project_v(s + 1)
                    if s >= 0:
                        times_v(s, k)
                    if k == 4 and 0 <= s + 1 < STAGES:
                        transpose_shift(s + 1)


def kernel(x, L0_conv_Wq, L0_conv_bq, L0_conv_Wk, L0_conv_bk, L0_conv_Wv, L0_conv_bv, L0_conv_gamma,
           L1_conv_wq, L1_conv_bq, L1_conv_wk, L1_conv_bk, L1_conv_wv, L1_conv_bv, L1_conv_gamma):
    import numpy as np
    import concourse.bacc as bacc
    from concourse.bass_utils import run_bass_kernel_spmd

    f32 = np.float32
    layers = [(L0_conv_Wq, L0_conv_bq, L0_conv_Wk, L0_conv_bk, L0_conv_Wv, L0_conv_bv, L0_conv_gamma),
              (L1_conv_wq, L1_conv_bq, L1_conv_wk, L1_conv_bk, L1_conv_wv, L1_conv_bv, L1_conv_gamma)]
    layers = [[np.asarray(a) for a in l] for l in layers]
    wqk = np.zeros((P, LAYERS, P), f32)
    wv = np.zeros((P, LAYERS, C), f32)
    columns = np.zeros((P, 2 * LAYERS + 1), f32)
    bv = np.zeros((P, LAYERS, C), f32)
    for l, (wq_l, bq_l, wk_l, bk_l, wv_l, bv_l, gamma_l) in enumerate(layers):
        for copy in range(3):
            rows = slice(copy * RD, (copy + 1) * RD)
            k_rows = slice(64 + copy * RD, 64 + (copy + 1) * RD)
            wqk[:, l, rows] = wq_l.T
            wqk[:, l, k_rows] = wk_l.T
            columns[rows, l] = bq_l
            columns[k_rows, l] = bk_l
        columns[64 + SHIFT_ROW:64 + SHIFT_ROW + 2, l] = 1.0
        columns[:, LAYERS + l] = gamma_l[0]
        wv[:, l] = wv_l.T
        bv[:, l] = bv_l[None, :]
    columns[2 * RD:3 * RD, 2 * LAYERS] = 1.0
    columns[64 + RD:64 + 2 * RD, 2 * LAYERS] = 1.0
    arrays = {
        "x_in": np.ascontiguousarray(np.asarray(x).reshape(B, C, N)),
        "wqk_in": wqk, "wv_in": wv, "columns_in": columns, "bv_in": bv,
        "identity_in": np.eye(P, dtype=f32),
    }
    nc = bacc.Bacc("TRN2", target_bir_lowering=False, num_devices=1)
    fp32 = mybir.dt.float32
    args = [nc.dram_tensor(name, a.shape, fp32, kind="ExternalInput").ap() for name, a in arrays.items()]
    out = nc.dram_tensor("out_dram", (B, C, N), fp32, kind="ExternalOutput").ap()
    build_attention_layers(nc, *args, out)
    r = run_bass_kernel_spmd(nc, [arrays], core_ids=[0])
    return r.results[0]["out_dram"].reshape(B, C, 32, 32)
```

```python
from contextlib import ExitStack

import concourse.bass as bass
from concourse import mybir

B, C, N, RD = 4, 128, 1024, 16
LAYERS = 2
STAGES = LAYERS * B
P = 128
TILES = N // P
HALF = N // 2
SHIFT_ROW = 3 * RD
NATIVE = 4
ORDER = [0, 4, 1, 5, 2, 6, 3, 7]
CUT = TILES - NATIVE
LEAD = 3
EARLY = 6
SHIFT_AT, V_AT, QK_AT, CUT_X_AT = 3, 5, 6, 2
QK_AHEAD = 3
RING = [("E", 1, 6), ("E", 1, 7), ("E", 2, 0), ("shift", 1, 0), ("E", 2, 1), ("E", 2, 2), ("E", 2, 3),
        ("V", 1, 0), ("E", 2, 4), ("QK", 3, 0), ("E", 2, 5)]
FIRST_STEP = -QK_AHEAD


def build_attention_layers(nc, x_in, wqk_in, wv_in, columns_in, bv_in, identity_in, out):
    fp32 = mybir.dt.float32
    fp32r = mybir.dt.float32r
    ALU = mybir.AluOpType
    ACT = mybir.ActivationFunctionType
    AX = mybir.AxisListType

    ctx = ExitStack()
    with ctx:
        def sb(name, shape, dt=fp32):
            return ctx.enter_context(nc.sbuf_tensor(name, shape, dt))

        def sem(name):
            return ctx.enter_context(nc.semaphore(name))

        x_all = sb("x_all", [P, STAGES + B, N])
        wqk = sb("wqk", [P, LAYERS, P])
        wv = sb("wv", [P, LAYERS, C])
        columns = sb("columns", [P, 2 * LAYERS + 1])
        bv_rows = sb("bv_rows", [P, LAYERS, C])
        identity = sb("identity", [P, P])
        wqk_hi = sb("wqk_hi", [P, LAYERS, P], fp32r)
        wqk_lo = sb("wqk_lo", [P, LAYERS, P], fp32r)
        x_hi = [sb(f"x_hi{p}", [P, N], fp32r) for p in range(2)]
        x_lo = [sb(f"x_lo{p}", [P, N], fp32r) for p in range(2)]
        masked_hi = sb("masked_hi", [P, N], fp32r)
        qk = [sb(f"qk{p}", [P, N], fp32r) for p in range(2)]
        qk_swapped = [sb(f"qk_swapped{p}", [P, N], fp32r) for p in range(2)]
        q_shifted = [sb(f"q_shifted{p}", [P, N], fp32r) for p in range(2)]
        k_twice = [sb(f"k_twice{p}", [P, N], fp32r) for p in range(2)]
        neg_max = [sb(f"neg_max{p}", [P, TILES]) for p in range(2)]
        row_sum = [sb(f"row_sum{p}", [P, TILES]) for p in range(2)]
        log_sum = [sb(f"log_sum{p}", [P, TILES]) for p in range(2)]
        shift = [sb(f"shift{p}", [P, TILES]) for p in range(2)]
        shift_parts = [sb(f"shift_parts{p}", [P, 2, TILES], fp32r) for p in range(2)]
        shift_rows = sb("shift_rows", [2 * TILES, P], fp32r)
        v32 = [sb(f"v32_{p}", [P, TILES, C]) for p in range(2)]
        v_hi = [sb(f"v_hi{p}", [P, CUT, C], fp32r) for p in range(2)]
        v_lo = [sb(f"v_lo{p}", [P, CUT, C], fp32r) for p in range(2)]
        attn = sb("attn", [P, TILES, N])
        attn_hi = sb("attn_hi", [P, CUT, N], fp32r)
        attn_lo = sb("attn_lo", [P, CUT, N], fp32r)

        e_ring = [ctx.enter_context(nc.psum_tensor(f"e_ring{i}", [P, N], fp32)) for i in range(2)]
        et_psum = ctx.enter_context(nc.psum_tensor("et_psum", [P, N], fp32))
        out_psum = ctx.enter_context(nc.psum_tensor("out_psum", [P, N], fp32))

        x_loaded = [sem(f"x_loaded{b}") for b in range(B)]
        wqk_loaded, wv_loaded, small_loaded = sem("wqk_loaded"), sem("wv_loaded"), sem("small_loaded")
        wqk_hi_made, wqk_cut = sem("wqk_hi_made"), sem("wqk_cut")
        x0_hi_made, x0_cut = sem("x0_hi_made"), sem("x0_cut")
        x_hi_made, x_cut = sem("x_hi_made"), sem("x_cut")
        qk_mm, masked_made, qk_made = sem("qk_mm"), sem("masked_made"), sem("qk_made")
        swapped, twice = sem("swapped"), sem("twice")
        v_mm, v32_made, v_hi_made, v_made = sem("v_mm"), sem("v32_made"), sem("v_hi_made"), sem("v_made")
        e_mm, max_made, sum_made = sem("e_mm"), sem("max_made"), sem("sum_made")
        log_made, shift_made, shift_mm = sem("log_made"), sem("shift_made"), sem("shift_mm")
        shift_hi_made, shift_cut = sem("shift_hi_made"), sem("shift_cut")
        shift_in_rows, shift_placed = sem("shift_in_rows"), sem("shift_placed")
        et_mm, attn_made = sem("et_mm"), sem("attn_made")
        attn_hi_made, attn_cut = sem("attn_hi_made"), sem("attn_cut")
        pv_mm, x_made, stored = sem("pv_mm"), sem("x_made"), sem("stored")

        block = ctx.enter_context(nc.Block())

        def at_least(engine, semaphore, value):
            if value > 0:
                engine.wait_ge(semaphore, value)

        def layer(s):
            return s // B

        def cut_before(k):
            return sum(j >= NATIVE for j in ORDER[:k])

        def e_tile(s, k):
            stage, i = (s + 1, k + EARLY) if k + EARLY < TILES else (s + 2, k + EARLY - TILES)
            return (stage, i) if 0 <= stage < STAGES else None

        def et_tile(s, k):
            stage, i = (s, k + LEAD) if k + LEAD < TILES else (s + 1, k + LEAD - TILES)
            return (stage, i) if 0 <= stage < STAGES else None

        def ring_slot(what, stage, i=0):
            turn, step = next((n, stage - ahead) for n, (w, ahead, tile) in enumerate(RING)
                              if (w, tile) == (what, i))
            return (len(RING) * step + turn) % 2

        def ring_wait(engine, what, stage, i=0):
            turn, step = next((n, stage - ahead) for n, (w, ahead, tile) in enumerate(RING)
                              if (w, tile) == (what, i))
            at = len(RING) * step + turn - 2
            while at >= len(RING) * FIRST_STEP:
                w, ahead, tile = RING[at % len(RING)]
                user = at // len(RING) + ahead
                if 0 <= user < STAGES:
                    if w == "E":
                        engine.wait_ge(sum_made, TILES * user + tile + 1)
                    else:
                        engine.wait_ge({"QK": qk_made, "V": v32_made, "shift": shift_in_rows}[w], user + 1)
                    return
                at -= 2

        @block.sync
        def _(sp):
            sp.dma_start(x_all[:, 0], x_in[0]).then_inc(x_loaded[0], 16)
            sp.dma_start(x_all[:, 1], x_in[1]).then_inc(x_loaded[1], 16)
            sp.dma_start(x_all[:, 2], x_in[2]).then_inc(x_loaded[2], 16)
            sp.dma_start(x_all[:, 3], x_in[3]).then_inc(x_loaded[3], 16)

            def swap_qk(s):
                sp.wait_ge(qk_made, s + 1)
                a, b = qk[s % 2][:].bitcast(fp32), qk_swapped[s % 2][:].bitcast(fp32)
                sp.dma_start(b[64:128, :], a[0:64, :]).then_inc(swapped, 16)
                sp.dma_start(b[0:64, :], a[64:128, :]).then_inc(swapped, 16)

            def copy_qk(s):
                sp.wait_ge(qk_made, s + 1)
                at_least(sp, et_mm, TILES * (s - 1))
                a, q2, k2 = (t[s % 2][:].bitcast(fp32) for t in (qk, q_shifted, k_twice))
                for half in (0, 64):
                    sp.dma_start(q2[half:half + 64, :], a[0:64, :]).then_inc(twice, 16)
                    sp.dma_start(k2[half:half + 64, :], a[64:128, :]).then_inc(twice, 16)

            def place_shift(s):
                sp.wait_ge(shift_in_rows, s + 1)
                sp.wait_ge(twice, 64 * (s + 1))
                for half in (0, 64):
                    rows = slice(half + SHIFT_ROW, half + SHIFT_ROW + 2)
                    to = q_shifted[s % 2][rows, :].bitcast(fp32).rearrange("a (i n) -> a i n", n=P)
                    sp.dma_start(to, shift_rows[:].bitcast(fp32)).then_inc(shift_placed, 16)

            def store(s):
                sp.wait_ge(x_made, 2 * (s + 1))
                sp.dma_start(out[s - B], x_all[:, s + B]).then_inc(stored, 16)

            for s in range(FIRST_STEP, STAGES):
                if s - 1 >= B:
                    store(s - 1)
                if 0 <= s + 1 < STAGES:
                    copy_qk(s + 1)
                    place_shift(s + 1)
                if s + QK_AHEAD < STAGES:
                    swap_qk(s + QK_AHEAD)
            store(STAGES - 1)
            sp.wait_ge(stored, 16 * B)

        @block.gpsimd
        def _(pool):
            def cut_x(s):
                p = s % 2
                if s < B:
                    pool.wait_ge(x_loaded[s], 16)
                else:
                    pool.wait_ge(x_made, 2 * (s - B + 1))
                at_least(pool, qk_mm, s - 1)
                nc.gpsimd.tensor_scalar(x_hi[p][:], x_all[:, s], 1.0, 0.0, ALU.mult,
                                        ALU.add).then_inc(x_hi_made, 1)
                pool.wait_ge(x_hi_made, s)
                nc.gpsimd.tensor_tensor(x_lo[p][:], x_all[:, s], x_hi[p][:].bitcast(fp32),
                                        ALU.subtract).then_inc(x_cut, 1)

            def cut_attn(s, k):
                j = ORDER[k]
                if j < NATIVE:
                    return
                pool.wait_ge(attn_made, TILES * s + k + 1)
                at_least(pool, pv_mm, TILES * (s - 1) + k + 1)
                nc.gpsimd.tensor_scalar(attn_hi[:, j - NATIVE], attn[:, j], 1.0, 0.0, ALU.mult,
                                        ALU.add).then_inc(attn_hi_made, 1)
                pool.wait_ge(attn_hi_made, CUT * s + cut_before(k) + 1)
                nc.gpsimd.tensor_tensor(attn_lo[:, j - NATIVE], attn[:, j],
                                        attn_hi[:, j - NATIVE].bitcast(fp32),
                                        ALU.subtract).then_inc(attn_cut, 1)

            for s in range(FIRST_STEP, STAGES):
                for k in range(TILES):
                    if et_tile(s, k):
                        cut_attn(*et_tile(s, k))
                    if k == CUT_X_AT and 0 < s + 3 < STAGES:
                        cut_x(s + 3)

        @block.scalar
        def _(act):
            act.preload_act_table_set("natural_log_exp_and_others")
            act.dma_start(wqk[:], wqk_in).then_inc(wqk_loaded, 16)
            act.dma_start(columns[:], columns_in).then_inc(small_loaded, 16)
            act.dma_start(identity[:], identity_in).then_inc(small_loaded, 16)
            act.dma_start(bv_rows[:], bv_in).then_inc(small_loaded, 16)
            act.dma_start(wv[:], wv_in).then_inc(wv_loaded, 16)

            def row_sums(s, i):
                act.wait_ge(max_made, TILES * s + i + 1)
                e = e_ring[ring_slot("E", s, i)]
                nc.scalar.activation(e[:], e[:], ACT.Exp, bias=neg_max[s % 2][:, i:i + 1],
                                     accum_out=row_sum[s % 2][:, i:i + 1]).then_inc(sum_made, 1)

            def log_sums(s):
                act.wait_ge(sum_made, TILES * (s + 1))
                nc.scalar.activation(log_sum[s % 2][:], row_sum[s % 2][:], ACT.Ln).then_inc(log_made, 1)

            def attention(s, k):
                j = ORDER[k]
                act.wait_ge(et_mm, TILES * s + k + 1)
                if j < NATIVE:
                    at_least(act, pv_mm, TILES * (s - 1) + k + 1)
                elif s > 0:
                    act.wait_ge(attn_cut, CUT * (s - 1) + cut_before(k) + 1)
                nc.scalar.activation(attn[:, j], et_psum[:], ACT.Exp).then_inc(attn_made, 1)

            for s in range(FIRST_STEP, STAGES):
                for k in range(TILES):
                    if et_tile(s, k):
                        attention(*et_tile(s, k))
                    if e_tile(s, k):
                        row_sums(*e_tile(s, k))
                    if k == TILES - EARLY - 1 and 0 <= s + 1 < STAGES:
                        log_sums(s + 1)

        @block.vector
        def _(dve):
            dve.wait_ge(wqk_loaded, 16)
            nc.vector.tensor_copy(wqk_hi[:], wqk[:]).then_inc(wqk_hi_made, 1)
            dve.wait_ge(wqk_hi_made, 1)
            nc.vector.tensor_tensor(wqk_lo[:], wqk[:], wqk_hi[:].bitcast(fp32),
                                    ALU.subtract).then_inc(wqk_cut, 1)
            dve.wait_ge(x_loaded[0], 16)
            nc.vector.tensor_copy(x_hi[0][:], x_all[:, 0]).then_inc(x0_hi_made, 1)
            dve.wait_ge(x0_hi_made, 1)
            nc.vector.tensor_tensor(x_lo[0][:], x_all[:, 0], x_hi[0][:].bitcast(fp32),
                                    ALU.subtract).then_inc(x0_cut, 1)
            dve.wait_ge(small_loaded, 48)

            def stack_qk(s):
                src, bias = e_ring[ring_slot("QK", s)], columns[:, layer(s):layer(s) + 1]
                mask = columns[:, 2 * LAYERS:2 * LAYERS + 1]
                dve.wait_ge(qk_mm, s + 1)
                at_least(dve, qk_made, s)
                nc.vector.tensor_scalar(masked_hi[:], src[:], bias, mask, ALU.add,
                                        ALU.mult).then_inc(masked_made, 1)
                dve.wait_ge(masked_made, s + 1)
                at_least(dve, e_mm, TILES * (s - 1))
                at_least(dve, swapped, 32 * (s - 1))
                at_least(dve, twice, 64 * (s - 1))
                nc.vector.scalar_tensor_tensor(out=qk[s % 2][:], in0=src[:], scalar=bias,
                                               in1=masked_hi[:].bitcast(fp32), op0=ALU.add,
                                               op1=ALU.subtract).then_inc(qk_made, 1)

            def make_v32(s):
                p, src = s % 2, e_ring[ring_slot("V", s)][:].rearrange("p (j c) -> p j c", c=C)
                bias = bv_rows[:, layer(s)][:, None, :].to_broadcast([P, TILES, C])
                dve.wait_ge(v_mm, s + 1)
                at_least(dve, pv_mm, TILES * (s - 1))
                nc.vector.tensor_tensor(v32[p][:], src, bias, ALU.add).then_inc(v32_made, 1)

            def cut_v(s):
                p = s % 2
                dve.wait_ge(v32_made, s + 1)
                nc.vector.tensor_copy(v_hi[p][:], v32[p][:, NATIVE:]).then_inc(v_hi_made, 1)
                dve.wait_ge(v_hi_made, s + 1)
                nc.vector.tensor_tensor(v_lo[p][:], v32[p][:, NATIVE:], v_hi[p][:].bitcast(fp32),
                                        ALU.subtract).then_inc(v_made, 1)

            def row_max(s, i):
                dve.wait_ge(e_mm, TILES * s + i + 1)
                nc.vector.tensor_reduce(neg_max[s % 2][:, i:i + 1], e_ring[ring_slot("E", s, i)][:], axis=AX.X,
                                        op=ALU.max, negate=True).then_inc(max_made, 1)

            def make_shift(s):
                p = s % 2
                dve.wait_ge(log_made, s + 1)
                dve.wait_ge(max_made, TILES * (s + 1))
                nc.vector.scalar_tensor_tensor(out=shift[p][:], in0=log_sum[p][:], scalar=-1.0,
                                               in1=neg_max[p][:], op0=ALU.mult,
                                               op1=ALU.add).then_inc(shift_made, 1)
                dve.wait_ge(shift_made, s + 1)
                nc.vector.tensor_copy(shift_parts[p][:, 0], shift[p][:]).then_inc(shift_hi_made, 1)
                dve.wait_ge(shift_hi_made, s + 1)
                nc.vector.tensor_tensor(shift_parts[p][:, 1], shift[p][:], shift_parts[p][:, 0].bitcast(fp32),
                                        ALU.subtract).then_inc(shift_cut, 1)

            def shift_to_rows(s):
                dve.wait_ge(shift_mm, s + 1)
                at_least(dve, shift_placed, 32 * s)
                nc.vector.tensor_copy(shift_rows[:], e_ring[ring_slot("shift", s)][0:2 * TILES, 0:P]
                                      ).then_inc(shift_in_rows, 1)

            def finish(s):
                dve.wait_ge(pv_mm, TILES * (s + 1))
                gamma = columns[:, LAYERS + layer(s):LAYERS + layer(s) + 1]
                for h in range(2):
                    part = slice(h * HALF, (h + 1) * HALF)
                    nc.vector.scalar_tensor_tensor(out=x_all[:, s + B, part], in0=out_psum[:, part],
                                                   scalar=gamma, in1=x_all[:, s, part], op0=ALU.mult,
                                                   op1=ALU.add).then_inc(x_made, 1)

            for s in range(FIRST_STEP, STAGES):
                if s - 1 >= 0:
                    finish(s - 1)
                for k in range(TILES):
                    if k == SHIFT_AT and 0 <= s + 1 < STAGES:
                        make_shift(s + 1)
                        shift_to_rows(s + 1)
                    if e_tile(s, k):
                        row_max(*e_tile(s, k))
                    if k == V_AT and 0 <= s + 1 < STAGES:
                        make_v32(s + 1)
                        cut_v(s + 1)
                    if k == QK_AT and s + QK_AHEAD < STAGES:
                        stack_qk(s + QK_AHEAD)
            finish(STAGES - 1)

        @block.tensor
        def _(pe):
            def project_qk(s):
                p, l, to = s % 2, layer(s), e_ring[ring_slot("QK", s)]
                if s == 0:
                    pe.wait_ge(wqk_cut, 1)
                    pe.wait_ge(x0_cut, 1)
                else:
                    pe.wait_ge(x_cut, s)
                ring_wait(pe, "QK", s)
                for n, (w, x) in enumerate(((wqk_hi, x_hi[p]), (wqk_hi, x_lo[p]), (wqk_lo, x_hi[p]))):
                    for h in range(2):
                        part = slice(h * HALF, (h + 1) * HALF)
                        last = nc.tensor.matmul(to[:, part], w[:, l, :], x[:, part], start=(n == 0),
                                                stop=(n == 2))
                last.then_inc(qk_mm, 1)

            def project_v(s):
                l, to = layer(s), e_ring[ring_slot("V", s)]
                if s == 0:
                    pe.wait_ge(wv_loaded, 16)
                if s < B:
                    pe.wait_ge(x_loaded[s], 16)
                else:
                    pe.wait_ge(x_made, 2 * (s - B + 1))
                ring_wait(pe, "V", s)
                for j in range(TILES):
                    last = nc.tensor.matmul(to[:, j * C:(j + 1) * C], x_all[:, s, j * P:(j + 1) * P], wv[:, l, :],
                                            start=True, stop=True)
                last.then_inc(v_mm, 1)

            def energies(s, i):
                p, to, rows = s % 2, e_ring[ring_slot("E", s, i)], slice(i * P, (i + 1) * P)
                if i == 0:
                    pe.wait_ge(swapped, 32 * (s + 1))
                ring_wait(pe, "E", s, i)
                nc.tensor.matmul(to[:, 0:HALF], qk[p][0:64, rows], qk_swapped[p][0:64, 0:HALF],
                                 start=True, stop=True)
                nc.tensor.matmul(to[:, HALF:N], qk_swapped[p][64:128, rows], qk[p][64:128, HALF:N],
                                 start=True, stop=True).then_inc(e_mm, 1)

            def transpose_shift(s):
                if s == 0:
                    pe.wait_ge(small_loaded, 48)
                ring_wait(pe, "shift", s)
                pe.wait_ge(shift_cut, s + 1)
                parts = shift_parts[s % 2][:].bitcast(fp32).rearrange("p a i -> p (a i)")
                nc.tensor.transpose(e_ring[ring_slot("shift", s)][0:2 * TILES, 0:P], parts,
                                    identity[:]).then_inc(shift_mm, 1)

            def energies_transposed(s, k):
                p, j = s % 2, ORDER[k]
                rows = slice(j * P, (j + 1) * P)
                if k == 0:
                    pe.wait_ge(shift_placed, 32 * (s + 1))
                at_least(pe, attn_made, TILES * s + k)
                nc.tensor.matmul(et_psum[:, 0:HALF], k_twice[p][0:64, rows], q_shifted[p][0:64, 0:HALF],
                                 start=True, stop=True)
                nc.tensor.matmul(et_psum[:, HALF:N], k_twice[p][64:128, rows],
                                 q_shifted[p][64:128, HALF:N], start=True, stop=True).then_inc(et_mm, 1)

            def times_v(s, k):
                p, j = s % 2, ORDER[k]
                if k == 0:
                    pe.wait_ge(v_made, s + 1)
                if j < NATIVE:
                    pe.wait_ge(attn_made, TILES * s + k + 1)
                    passes = ((v32[p][:, j], attn[:, j]),)
                else:
                    pe.wait_ge(attn_cut, CUT * s + cut_before(k) + 1)
                    c = j - NATIVE
                    passes = ((v_hi[p][:, c], attn_hi[:, c]), (v_hi[p][:, c], attn_lo[:, c]),
                              (v_lo[p][:, c], attn_hi[:, c]))
                for n, (v, a) in enumerate(passes):
                    for h in range(2):
                        part = slice(h * HALF, (h + 1) * HALF)
                        if k == 0 and n == 0:
                            at_least(pe, x_made, 2 * (s - 1) + h + 1)
                        last = nc.tensor.matmul(out_psum[:, part], v, a[:, part],
                                                start=(k == 0 and n == 0),
                                                stop=(k == TILES - 1 and n == len(passes) - 1))
                last.then_inc(pv_mm, 1)

            for s in range(FIRST_STEP, STAGES):
                for k in range(TILES):
                    if et_tile(s, k):
                        energies_transposed(*et_tile(s, k))
                    if k == SHIFT_AT and 0 <= s + 1 < STAGES:
                        transpose_shift(s + 1)
                    if e_tile(s, k):
                        energies(*e_tile(s, k))
                    if s >= 0:
                        times_v(s, k)
                    if k == V_AT and 0 <= s + 1 < STAGES:
                        project_v(s + 1)
                    if k == QK_AT and s + QK_AHEAD < STAGES:
                        project_qk(s + QK_AHEAD)


def kernel(x, L0_conv_Wq, L0_conv_bq, L0_conv_Wk, L0_conv_bk, L0_conv_Wv, L0_conv_bv, L0_conv_gamma,
           L1_conv_wq, L1_conv_bq, L1_conv_wk, L1_conv_bk, L1_conv_wv, L1_conv_bv, L1_conv_gamma):
    import numpy as np
    import concourse.bacc as bacc
    from concourse.bass_utils import run_bass_kernel_spmd

    f32 = np.float32
    layers = [(L0_conv_Wq, L0_conv_bq, L0_conv_Wk, L0_conv_bk, L0_conv_Wv, L0_conv_bv, L0_conv_gamma),
              (L1_conv_wq, L1_conv_bq, L1_conv_wk, L1_conv_bk, L1_conv_wv, L1_conv_bv, L1_conv_gamma)]
    layers = [[np.asarray(a) for a in l] for l in layers]
    wqk = np.zeros((P, LAYERS, P), f32)
    wv = np.zeros((P, LAYERS, C), f32)
    columns = np.zeros((P, 2 * LAYERS + 1), f32)
    bv = np.zeros((P, LAYERS, C), f32)
    for l, (wq_l, bq_l, wk_l, bk_l, wv_l, bv_l, gamma_l) in enumerate(layers):
        for copy in range(3):
            rows = slice(copy * RD, (copy + 1) * RD)
            k_rows = slice(64 + copy * RD, 64 + (copy + 1) * RD)
            wqk[:, l, rows] = wq_l.T
            wqk[:, l, k_rows] = wk_l.T
            columns[rows, l] = bq_l
            columns[k_rows, l] = bk_l
        columns[64 + SHIFT_ROW:64 + SHIFT_ROW + 2, l] = 1.0
        columns[:, LAYERS + l] = gamma_l[0]
        wv[:, l] = wv_l.T
        bv[:, l] = bv_l[None, :]
    columns[2 * RD:3 * RD, 2 * LAYERS] = 1.0
    columns[64 + RD:64 + 2 * RD, 2 * LAYERS] = 1.0
    arrays = {
        "x_in": np.ascontiguousarray(np.asarray(x).reshape(B, C, N)),
        "wqk_in": wqk, "wv_in": wv, "columns_in": columns, "bv_in": bv,
        "identity_in": np.eye(P, dtype=f32),
    }
    nc = bacc.Bacc("TRN2", target_bir_lowering=False, num_devices=1)
    fp32 = mybir.dt.float32
    args = [nc.dram_tensor(name, a.shape, fp32, kind="ExternalInput").ap() for name, a in arrays.items()]
    out = nc.dram_tensor("out_dram", (B, C, N), fp32, kind="ExternalOutput").ap()
    build_attention_layers(nc, *args, out)
    r = run_bass_kernel_spmd(nc, [arrays], core_ids=[0])
    return r.results[0]["out_dram"].reshape(B, C, 32, 32)
```

```python
from contextlib import ExitStack

from concourse import mybir

B, C, N, RD = 4, 128, 1024, 16
LAYERS = 2
STAGES = LAYERS * B
P = 128
TILES = N // P
HALF = N // 2
SHIFT_ROW = 3 * RD
NATIVE = 2
ORDER = [0, 2, 3, 4, 5, 6, 7, 1]
HI_BY_SCALAR = (2, 4, 6)
LAST_BY_VECTOR = (1, 3, 6)
CUT = TILES - NATIVE
RING = 3
WARM_UP = 8
KEEP_WARM = (0, 0, 2, 2, 2, 2, 2, 2, 2, 2, 2, 2, 2, 2, 2, 2, 2, 2, 2, 2, 2, 2, 2, 2, 2)
QK_SETS = 3
GAMMA, MASK, SWAPPED_BIAS, SWAPPED_MASK, SHIFT_MASK, COLUMNS = 2, 4, 5, 6, 7, 8
IDENTITY, LATE = 2 * LAYERS, 2 * LAYERS + 2

PE_FIRST = [
    ("QK", 0, 0), ("QK swapped", 0, 0), ("V", 0, 0), ("E", 0, 0), ("E", 0, 1), ("QK", 1, 0), ("E", 0, 2),
    ("E", 0, 3), ("E", 0, 4), ("E", 0, 5), ("E", 0, 6), ("E", 0, 7), ("E", 1, 0), ("E", 1, 1), ("E", 1, 2),
    ("shift", 0, 0), ("E", 1, 3), ("E", 1, 4), ("ET", 0, 0), ("ET", 0, 1), ("E", 1, 5), ("E", 1, 6),
    ("QK", 2, 0), ("ET", 0, 2), ("PV", 0, 0), ("ET", 0, 3), ("ET", 0, 4), ("E", 1, 7), ("V", 1, 0),
    ("ET", 0, 5), ("ET", 0, 6), ("shift", 1, 0), ("ET", 0, 7), ("E", 2, 0), ("E", 2, 1), ("PV", 0, 1),
    ("E", 2, 2), ("PV", 0, 2), ("E", 2, 3),
]
PE_STEP = [
    ("QK", 3, 0), ("PV", 0, 3), ("ET", 1, 0), ("ET", 1, 1), ("PV", 0, 4), ("ET", 1, 2), ("ET", 1, 3),
    ("E", 2, 4), ("PV", 0, 5), ("ET", 1, 4), ("E", 2, 5), ("PV", 0, 6), ("E", 2, 6), ("E", 2, 7),
    ("PV", 0, 7), ("V", 2, 0), ("ET", 1, 5), ("ET", 1, 6), ("PV", 1, 0), ("shift", 2, 0), ("ET", 1, 7),
    ("E", 3, 0), ("E", 3, 1), ("PV", 1, 1), ("E", 3, 2), ("PV", 1, 2), ("E", 3, 3),
]
ACT_FIRST = [
    ("sum", 0, 0), ("v_hi", 0, 0), ("sum", 0, 1), ("sum", 0, 2), ("sum", 0, 3), ("sum", 0, 4),
    ("sum", 0, 5), ("sum", 0, 6), ("sum", 0, 7), ("log", 0, 0), ("sum", 1, 0), ("sum", 1, 1), ("sum", 1, 2),
    ("sum", 1, 3), ("sum", 1, 4), ("attn", 0, 0), ("attn", 0, 1), ("sum", 1, 5), ("sum", 1, 6),
    ("attn", 0, 2), ("hi", 0, 2), ("attn", 0, 3), ("attn", 0, 4), ("sum", 1, 7), ("log", 1, 0),
    ("attn", 0, 5), ("attn", 0, 6), ("hi", 0, 4), ("attn", 0, 7), ("sum", 2, 0), ("sum", 2, 1),
    ("hi", 0, 6), ("sum", 2, 2), ("sum", 2, 3), ("v_hi", 1, 0), ("attn", 1, 0), ("attn", 1, 1),
    ("attn", 1, 2), ("attn", 1, 3), ("sum", 2, 4),
]
ACT_STEP = [
    ("attn", 1, 4), ("hi", 1, 2), ("sum", 2, 5), ("sum", 2, 6), ("sum", 2, 7), ("log", 2, 0), ("hi", 1, 4),
    ("attn", 1, 5), ("attn", 1, 6), ("hi", 1, 6), ("attn", 1, 7), ("v_hi", 2, 0), ("sum", 3, 0),
    ("sum", 3, 1), ("sum", 3, 2), ("sum", 3, 3), ("attn", 2, 0), ("attn", 2, 1), ("attn", 2, 2),
    ("attn", 2, 3), ("sum", 3, 4),
]
DVE_FIRST = [
    ("v32", 0, 0), ("max", 0, 0), ("max", 0, 1),
    ("mask", 1, 0), ("max", 0, 2), ("stack", 1, 0), ("max", 0, 3), ("max", 0, 4), ("max", 0, 5),
    ("max", 0, 6), ("max", 0, 7), ("max", 1, 0), ("max", 1, 1), ("max", 1, 2), ("rows", 0, 0),
    ("max", 1, 3), ("max", 1, 4), ("v_lo", 0, 0), ("max", 1, 5), ("max", 1, 6), ("mask", 2, 0),
    ("stack", 2, 0), ("max", 1, 7),
]
DVE_STEP = [
    ("v32", 1, 0), ("cut", 0, 3), ("rows", 1, 0), ("max", 2, 0), ("cut", 0, 6), ("max", 2, 1),
    ("max", 2, 2), ("max", 2, 3), ("mask", 3, 0), ("cut", 1, 1), ("stack", 3, 0), ("max", 2, 4),
    ("v_lo", 1, 0), ("max", 2, 5), ("max", 2, 6), ("max", 2, 7), ("finish", 0, 0), ("finish", 0, 1),
]
POOL_FIRST = [
    ("x", 1, 0), ("x", 2, 0), ("cut", 0, 1), ("cut", 0, 2),
]
POOL_STEP = [
    ("x", 3, 0), ("cut", 0, 3), ("cut", 0, 4), ("cut", 0, 5), ("cut", 0, 6), ("cut", 1, 1), ("cut", 1, 2),
]
SP_FIRST = [
    ("copy", 0, 0), ("swap", 1, 0), ("place", 0, 0), ("swap", 2, 0), ("copy", 1, 0), ("place", 1, 0),
]
SP_STEP = [
    ("swap", 3, 0), ("copy", 2, 0), ("place", 2, 0), ("store", -1, 0),
]


def in_order(first, step):
    yield from first
    for s in range(STAGES + 1):
        for what, ahead, i in step:
            if (B if what == "store" else 0) <= s + ahead < STAGES:
                yield what, s + ahead, i


def build_attention_layers(nc, x_in, weights_in, late_in, out):
    fp32 = mybir.dt.float32
    fp32r = mybir.dt.float32r
    ALU = mybir.AluOpType
    ACT = mybir.ActivationFunctionType
    AX = mybir.AxisListType

    ctx = ExitStack()
    with ctx:
        def sb(name, shape, dt=fp32):
            return ctx.enter_context(nc.sbuf_tensor(name, shape, dt))

        def sem(name):
            return ctx.enter_context(nc.semaphore(name))

        x_all = sb("x_all", [P, STAGES, N])
        weights = sb("weights", [P, QK_SETS * P + COLUMNS])
        late = sb("late", [P, LATE, P])
        wqk_hi = sb("wqk_hi", [P, QK_SETS * P], fp32r)
        wqk_lo = sb("wqk_lo", [P, QK_SETS * P], fp32r)
        x_hi = [sb(f"x_hi{p}", [P, N], fp32r) for p in range(2)]
        x_lo = [sb(f"x_lo{p}", [P, N], fp32r) for p in range(2)]
        masked_hi = sb("masked_hi", [P, N], fp32r)
        qk = [sb(f"qk{p}", [P, N], fp32r) for p in range(2)]
        qk_swapped = [sb(f"qk_swapped{p}", [P, N], fp32r) for p in range(2)]
        q_shifted = [sb(f"q_shifted{p}", [P, N], fp32r) for p in range(2)]
        k_twice = [sb(f"k_twice{p}", [P, N], fp32r) for p in range(2)]
        neg_max = [sb(f"neg_max{p}", [P, 2 * TILES]) for p in range(2)]
        row_sum = [sb(f"row_sum{p}", [P, TILES]) for p in range(2)]
        log_sum = [sb(f"log_sum{p}", [P, 2 * TILES]) for p in range(2)]
        zeros = sb("zeros", [P, HALF], mybir.dt.bfloat16)
        shift_rows = sb("shift_rows", [2 * TILES, P], fp32r)
        shift_masked = sb("shift_masked", [2 * TILES, P], fp32r)
        v32 = [sb(f"v32_{p}", [P, TILES, C]) for p in range(2)]
        v_hi = [sb(f"v_hi{p}", [P, CUT, C], fp32r) for p in range(2)]
        v_lo = [sb(f"v_lo{p}", [P, CUT, C], fp32r) for p in range(2)]
        attn = sb("attn", [P, TILES, N])
        attn_hi = sb("attn_hi", [P, CUT, N], fp32r)
        attn_lo = sb("attn_lo", [P, CUT, N], fp32r)

        ring = [ctx.enter_context(nc.psum_tensor(f"ring{i}", [P, N], fp32)) for i in range(RING)]
        out_psum = ctx.enter_context(nc.psum_tensor("out_psum", [P, N], fp32))

        x_loaded = {b: sem(f"x_loaded{b}") for b in range(1, B)}
        x0_loaded, x0_lo_made = [sem(f"x0_loaded{h}") for h in range(2)], [sem(f"x0_lo_made{h}") for h in range(2)]
        weights_loaded, late_loaded = sem("weights_loaded"), sem("late_loaded")
        wqk_hi_made, wqk_cut = sem("wqk_hi_made"), sem("wqk_cut")
        x0_hi_made, qk0_mm = sem("x0_hi_made"), sem("qk0_mm")
        x_hi_made, x_cut = sem("x_hi_made"), sem("x_cut")
        qk_mm, masked_made, qk_made = sem("qk_mm"), sem("masked_made"), sem("qk_made")
        biased0_made, masked0_made, stacked0_made = sem("biased0_made"), sem("masked0_made"), sem("stacked0_made")
        zeros_made = sem("zeros_made")
        swapped, twice = [sem(f"swapped{p}") for p in range(2)], [sem(f"twice{p}") for p in range(2)]
        v_mm, v32_made, v_hi_made, v_made = sem("v_mm"), sem("v32_made"), sem("v_hi_made"), sem("v_made")
        e_mm, max_made, sum_made = sem("e_mm"), sem("max_made"), sem("sum_made")
        max_twice, log_made, shift_mm = sem("max_twice"), sem("log_made"), sem("shift_mm")
        shift_hi_made, shift_in_rows, shift_placed = sem("shift_hi_made"), sem("shift_in_rows"), sem("shift_placed")
        et_mm, attn_made = sem("et_mm"), sem("attn_made")
        hi_made = {engine: sem(f"hi_made_{engine}") for engine in ("vector", "scalar", "gpsimd")}
        lo_made = {engine: sem(f"lo_made_{engine}") for engine in ("vector", "gpsimd")}
        pv_half_mm, pv_mm, x_made, stored = sem("pv_half_mm"), sem("pv_mm"), sem("x_made"), sem("stored")

        block = ctx.enter_context(nc.Block())

        def at_least(engine, semaphore, value):
            if value > 0:
                engine.wait_ge(semaphore, value)

        def layer(s):
            return s // B

        def hi_on(s, k):
            if ORDER[k] < NATIVE:
                return None
            if s == STAGES - 1 and k in LAST_BY_VECTOR:
                return "vector"
            return "scalar" if k in HI_BY_SCALAR else "gpsimd"

        def lo_on(s, k):
            if ORDER[k] < NATIVE:
                return None
            return "vector" if s == STAGES - 1 and k in LAST_BY_VECTOR else "gpsimd"

        hi_turns = {"vector": [(s, k) for what, s, k in in_order(DVE_FIRST, DVE_STEP)
                               if what == "cut" and lo_on(s, k) == "vector"],
                    "scalar": [(s, k) for what, s, k in in_order(ACT_FIRST, ACT_STEP)
                               if what == "hi" and hi_on(s, k) == "scalar"],
                    "gpsimd": [(s, k) for what, s, k in in_order(POOL_FIRST, POOL_STEP)
                               if what == "cut" and hi_on(s, k) == "gpsimd"]}
        lo_turns = {"vector": [(s, k) for what, s, k in in_order(DVE_FIRST, DVE_STEP)
                               if what == "cut" and lo_on(s, k) == "vector"],
                    "gpsimd": [(s, k) for what, s, k in in_order(POOL_FIRST, POOL_STEP)
                               if what == "cut" and lo_on(s, k) == "gpsimd"]}

        def wait_for_hi(engine, s, k):
            by = hi_on(s, k)
            engine.wait_ge(hi_made[by], hi_turns[by].index((s, k)) + 1)

        def wait_for_lo(engine, s, k):
            by = lo_on(s, k)
            engine.wait_ge(lo_made[by], lo_turns[by].index((s, k)) + 1)

        turns = [use for use in in_order(PE_FIRST, PE_STEP) if use[0] != "PV"]

        def ring_tile(*use):
            return ring[turns.index(use) % RING]

        def stacked(s):
            return (stacked0_made, 2) if s == 0 else (qk_made, s)

        def wait_for_ring(engine, *use):
            turn = turns.index(use)
            if turn < RING:
                return
            what, s, i = turns[turn - RING]
            if what == "ET":
                engine.wait_ge(attn_made, TILES * s + i + 1)
            elif what == "E":
                engine.wait_ge(sum_made, TILES * s + i + 1)
            elif what == "V":
                engine.wait_ge(v32_made, s + 1)
            elif what == "QK":
                engine.wait_ge(*stacked(s))
            elif what == "QK swapped":
                engine.wait_ge(stacked0_made, 4)
            else:
                engine.wait_ge(shift_in_rows, s + 1)

        @block.sync
        def _(sp):
            sp.dma_start(weights[:], weights_in).then_inc(weights_loaded, 16)
            for h in range(2):
                part = slice(h * HALF, (h + 1) * HALF)
                sp.dma_start(x_all[:, 0, part], x_in[0, :, part]).then_inc(x0_loaded[h], 16)
            sp.dma_start(x_all[:, 1], x_in[1]).then_inc(x_loaded[1], 16)
            sp.dma_start(late[:], late_in).then_inc(late_loaded, 16)
            sp.dma_start(x_all[:, 2], x_in[2]).then_inc(x_loaded[2], 16)
            sp.dma_start(x_all[:, 3], x_in[3]).then_inc(x_loaded[3], 16)

            def swap_qk(s):
                sp.wait_ge(*stacked(s))
                a, b = qk[s % 2][:].bitcast(fp32), qk_swapped[s % 2][:].bitcast(fp32)
                sp.dma_start(b[64:128, :], a[0:64, :]).then_inc(swapped[s % 2], 16)
                sp.dma_start(b[0:64, :], a[64:128, :]).then_inc(swapped[s % 2], 16)

            def copy_qk(s):
                sp.wait_ge(*stacked(s))
                at_least(sp, et_mm, TILES * (s - 1))
                a, q2, k2 = (t[s % 2][:].bitcast(fp32) for t in (qk, q_shifted, k_twice))
                for half in (0, 64):
                    sp.dma_start(q2[half:half + 64, :], a[0:64, :]).then_inc(twice[s % 2], 16)
                    sp.dma_start(k2[half:half + 64, :], a[64:128, :]).then_inc(twice[s % 2], 16)

            def place_shift(s):
                sp.wait_ge(shift_in_rows, s + 1)
                sp.wait_ge(twice[s % 2], 64 * (s // 2 + 1))
                for half in (0, 64):
                    rows = slice(half + SHIFT_ROW, half + SHIFT_ROW + 2)
                    to = q_shifted[s % 2][rows, :].bitcast(fp32).rearrange("a (i n) -> a i n", n=P)
                    sp.dma_start(to, shift_rows[:].bitcast(fp32)).then_inc(shift_placed, 16)

            def store(s):
                for h in range(2):
                    part = slice(h * HALF, (h + 1) * HALF)
                    sp.wait_ge(x_made, 2 * s + h + 1)
                    sp.dma_start(out[s - B, :, part], x_all[:, s, part]).then_inc(stored, 16)

            for what, s, _i in in_order(SP_FIRST, SP_STEP):
                if what == "copy":
                    copy_qk(s)
                elif what == "place":
                    place_shift(s)
                elif what == "swap" and s > 0:
                    swap_qk(s)
                elif what == "store":
                    store(s)
            sp.wait_ge(stored, 32 * B)

        @block.gpsimd
        def _(pool):
            nc.gpsimd.memset(zeros[:], 0.0).then_inc(zeros_made, 1)
            pool.wait_ge(x0_hi_made, 1)
            nc.gpsimd.tensor_tensor(x_lo[0][:, 0:HALF], x_all[:, 0, 0:HALF], x_hi[0][:, 0:HALF].bitcast(fp32),
                                    ALU.subtract).then_inc(x0_lo_made[0], 1)

            def cut_x(s):
                if s < B:
                    pool.wait_ge(x_loaded[s], 16)
                else:
                    pool.wait_ge(x_made, 2 * (s - B + 1))
                if s == 2:
                    pool.wait_ge(qk0_mm, 4)
                at_least(pool, qk_mm, s - 2)
                nc.gpsimd.tensor_scalar(x_hi[s % 2][:], x_all[:, s], 1.0, 0.0, ALU.mult,
                                        ALU.add).then_inc(x_hi_made, 1)
                pool.wait_ge(x_hi_made, s)
                nc.gpsimd.tensor_tensor(x_lo[s % 2][:], x_all[:, s], x_hi[s % 2][:].bitcast(fp32),
                                        ALU.subtract).then_inc(x_cut, 1)

            def attn_hi_of(s, k):
                j = ORDER[k]
                pool.wait_ge(attn_made, TILES * s + k + 1)
                at_least(pool, pv_mm, TILES * (s - 1) + k + 1)
                nc.gpsimd.tensor_scalar(attn_hi[:, j - NATIVE], attn[:, j], 1.0, 0.0, ALU.mult,
                                        ALU.add).then_inc(hi_made["gpsimd"], 1)

            def attn_lo_of(s, k):
                j = ORDER[k]
                wait_for_hi(pool, s, k)
                nc.gpsimd.tensor_tensor(attn_lo[:, j - NATIVE], attn[:, j],
                                        attn_hi[:, j - NATIVE].bitcast(fp32),
                                        ALU.subtract).then_inc(lo_made["gpsimd"], 1)

            for what, s, i in in_order(POOL_FIRST, POOL_STEP):
                if what == "x":
                    cut_x(s)
                elif lo_on(s, i) == "gpsimd":
                    if hi_on(s, i) == "gpsimd":
                        attn_hi_of(s, i)
                    attn_lo_of(s, i)

        @block.scalar
        def _(act):
            act.preload_act_table_set("natural_log_exp_and_others")

            def add_bias0():
                act.wait_ge(weights_loaded, 16)
                for n, (use, bias) in enumerate((("QK", 0), ("QK swapped", SWAPPED_BIAS))):
                    for h in range(2):
                        part = slice(h * HALF, (h + 1) * HALF)
                        act.wait_ge(qk0_mm, 2 * n + h + 1)
                        nc.scalar.activation(attn[:, n, part], ring_tile(use, 0, 0)[:, part], ACT.Identity,
                                             bias=weights[:, QK_SETS * P + bias:QK_SETS * P + bias + 1]
                                             ).then_inc(biased0_made, 1)

            def row_sums(s, i):
                act.wait_ge(max_made, TILES * s + i + 1)
                e = ring_tile("E", s, i)
                nc.scalar.activation(e[:], e[:], ACT.Exp, bias=neg_max[s % 2][:, i:i + 1],
                                     accum_out=row_sum[s % 2][:, i:i + 1]).then_inc(sum_made, 1)

            def log_sums(s):
                p = s % 2
                act.wait_ge(max_made, TILES * (s + 1))
                nc.scalar.copy(neg_max[p][:, TILES:], neg_max[p][:, 0:TILES]).then_inc(max_twice, 1)
                act.wait_ge(sum_made, TILES * (s + 1))
                sums = row_sum[p][:][:, None, :].to_broadcast([P, 2, TILES])
                nc.scalar.activation(log_sum[p][:].rearrange("p (a i) -> p a i", a=2), sums,
                                     ACT.Ln).then_inc(log_made, 1)

            def attention(s, k):
                j = ORDER[k]
                act.wait_ge(et_mm, TILES * s + k + 1)
                if j < NATIVE:
                    at_least(act, pv_mm, TILES * (s - 1) + k + 1)
                elif s > 0:
                    wait_for_lo(act, s - 1, k)
                nc.scalar.activation(attn[:, j], ring_tile("ET", s, k)[:], ACT.Exp).then_inc(attn_made, 1)

            def attn_hi_of(s, k):
                j = ORDER[k]
                act.wait_ge(attn_made, TILES * s + k + 1)
                at_least(act, pv_mm, TILES * (s - 1) + k + 1)
                nc.scalar.copy(attn_hi[:, j - NATIVE], attn[:, j]).then_inc(hi_made["scalar"], 1)

            def make_v_hi(s):
                act.wait_ge(v32_made, s + 1)
                nc.scalar.copy(v_hi[s % 2][:], v32[s % 2][:, NATIVE:]).then_inc(v_hi_made, 1)

            add_bias0()
            for what, s, i in in_order(ACT_FIRST, ACT_STEP):
                if what == "attn":
                    attention(s, i)
                elif what == "sum":
                    row_sums(s, i)
                elif what == "hi":
                    if hi_on(s, i) == "scalar":
                        attn_hi_of(s, i)
                elif what == "v_hi":
                    make_v_hi(s)
                else:
                    log_sums(s)

        @block.vector
        def _(dve):
            columns = weights[:, QK_SETS * P:]
            dve.wait_ge(weights_loaded, 16)
            nc.vector.tensor_copy(wqk_hi[:], weights[:, 0:QK_SETS * P]).then_inc(wqk_hi_made, 1)
            dve.wait_ge(wqk_hi_made, 1)
            nc.vector.tensor_tensor(wqk_lo[:], weights[:, 0:QK_SETS * P], wqk_hi[:].bitcast(fp32),
                                    ALU.subtract).then_inc(wqk_cut, 1)
            for h in range(2):
                part = slice(h * HALF, (h + 1) * HALF)
                dve.wait_ge(x0_loaded[h], 16)
                nc.vector.tensor_copy(x_hi[0][:, part], x_all[:, 0, part]).then_inc(x0_hi_made, 1)
            dve.wait_ge(x0_hi_made, 2)
            nc.vector.tensor_tensor(x_lo[0][:, HALF:], x_all[:, 0, HALF:], x_hi[0][:, HALF:].bitcast(fp32),
                                    ALU.subtract).then_inc(x0_lo_made[1], 1)

            for n, (mask, to) in enumerate(((MASK, qk[0]), (SWAPPED_MASK, qk_swapped[0]))):
                for h in range(2):
                    part = slice(h * HALF, (h + 1) * HALF)
                    dve.wait_ge(biased0_made, 2 * n + h + 1)
                    if n == 1:
                        dve.wait_ge(stacked0_made, h + 1)
                    nc.vector.tensor_scalar(masked_hi[:, part], attn[:, n, part], columns[:, mask:mask + 1], 0.0,
                                            ALU.mult, ALU.add).then_inc(masked0_made, 1)
                for h in range(2):
                    part = slice(h * HALF, (h + 1) * HALF)
                    dve.wait_ge(masked0_made, 2 * n + h + 1)
                    nc.vector.tensor_tensor(to[:, part], attn[:, n, part], masked_hi[:, part].bitcast(fp32),
                                            ALU.subtract).then_inc(stacked0_made, 1)

            def mask_qk(s):
                dve.wait_ge(qk_mm, s)
                dve.wait_ge(*((stacked0_made, 4) if s == 1 else (qk_made, s - 1)))
                nc.vector.tensor_scalar(masked_hi[:], ring_tile("QK", s, 0)[:], columns[:, layer(s):layer(s) + 1],
                                        columns[:, MASK:MASK + 1], ALU.add, ALU.mult).then_inc(masked_made, 1)

            def stack_qk(s):
                dve.wait_ge(masked_made, s)
                at_least(dve, e_mm, TILES * (s - 1))
                at_least(dve, swapped[s % 2], 32 * ((s - 1) // 2))
                at_least(dve, twice[s % 2], 64 * (s // 2))
                nc.vector.scalar_tensor_tensor(out=qk[s % 2][:], in0=ring_tile("QK", s, 0)[:],
                                               scalar=columns[:, layer(s):layer(s) + 1],
                                               in1=masked_hi[:].bitcast(fp32), op0=ALU.add,
                                               op1=ALU.subtract).then_inc(qk_made, 1)

            def make_v32(s):
                p, src = s % 2, ring_tile("V", s, 0)[:].rearrange("p (j c) -> p j c", c=C)
                bias = late[:, LAYERS + layer(s)][:, None, :].to_broadcast([P, TILES, C])
                if s == 0:
                    dve.wait_ge(late_loaded, 16)
                dve.wait_ge(v_mm, s + 1)
                at_least(dve, pv_mm, TILES * (s - 1))
                nc.vector.tensor_tensor(v32[p][:], src, bias, ALU.add).then_inc(v32_made, 1)

            def make_v_lo(s):
                p = s % 2
                dve.wait_ge(v_hi_made, s + 1)
                nc.vector.tensor_tensor(v_lo[p][:], v32[p][:, NATIVE:], v_hi[p][:].bitcast(fp32),
                                        ALU.subtract).then_inc(v_made, 1)

            def row_max(s, i):
                dve.wait_ge(e_mm, TILES * s + i + 1)
                nc.vector.tensor_reduce(neg_max[s % 2][:, i:i + 1], ring_tile("E", s, i)[:], axis=AX.X,
                                        op=ALU.max, negate=True).then_inc(max_made, 1)

            def shift_to_rows(s):
                src = ring_tile("shift", s, 0)[0:2 * TILES, 0:P]
                dve.wait_ge(shift_mm, s + 1)
                at_least(dve, shift_in_rows, s)
                nc.vector.tensor_scalar(shift_masked[:], src, columns[0:2 * TILES, SHIFT_MASK:SHIFT_MASK + 1], None,
                                        ALU.mult).then_inc(shift_hi_made, 1)
                dve.wait_ge(shift_hi_made, s + 1)
                at_least(dve, shift_placed, 32 * s)
                nc.vector.tensor_tensor(shift_rows[:], src, shift_masked[:].bitcast(fp32),
                                        ALU.subtract).then_inc(shift_in_rows, 1)

            def attn_hi_of(s, k):
                j = ORDER[k]
                dve.wait_ge(attn_made, TILES * s + k + 1)
                at_least(dve, pv_mm, TILES * (s - 1) + k + 1)
                nc.vector.tensor_copy(attn_hi[:, j - NATIVE], attn[:, j]).then_inc(hi_made["vector"], 1)

            def attn_lo_of(s, k):
                j = ORDER[k]
                wait_for_hi(dve, s, k)
                nc.vector.tensor_tensor(attn_lo[:, j - NATIVE], attn[:, j],
                                        attn_hi[:, j - NATIVE].bitcast(fp32),
                                        ALU.subtract).then_inc(lo_made["vector"], 1)

            def finish(s, h):
                dve.wait_ge(pv_half_mm if h == 0 else pv_mm, s + 1 if h == 0 else TILES * (s + 1))
                gamma, part = columns[:, GAMMA + layer(s):GAMMA + layer(s) + 1], slice(h * HALF, (h + 1) * HALF)
                nc.vector.scalar_tensor_tensor(out=x_all[:, s + B if s < B else s, part], in0=out_psum[:, part],
                                               scalar=gamma, in1=x_all[:, s, part], op0=ALU.mult,
                                               op1=ALU.add).then_inc(x_made, 1)

            for what, s, i in in_order(DVE_FIRST, DVE_STEP):
                if what == "max":
                    row_max(s, i)
                elif what == "mask":
                    mask_qk(s)
                elif what == "stack":
                    stack_qk(s)
                elif what == "cut":
                    if lo_on(s, i) == "vector":
                        attn_hi_of(s, i)
                        attn_lo_of(s, i)
                elif what == "v32":
                    make_v32(s)
                elif what == "v_lo":
                    make_v_lo(s)
                elif what == "rows":
                    shift_to_rows(s)
                else:
                    finish(s, i)

        @block.tensor
        def _(pe):
            def project_qk0():
                pe.wait_ge(wqk_cut, 1)
                for n, use in enumerate(("QK", "QK swapped")):
                    w, to = slice(n * P, (n + 1) * P), ring_tile(use, 0, 0)
                    for h in range(2):
                        part = slice(h * HALF, (h + 1) * HALF)
                        if n == 0:
                            pe.wait_ge(x0_hi_made, h + 1)
                        nc.tensor.matmul(to[:, part], wqk_hi[:, w], x_hi[0][:, part], start=True, stop=False)
                        nc.tensor.matmul(to[:, part], wqk_lo[:, w], x_hi[0][:, part], start=False, stop=False)
                    for h in range(2):
                        part = slice(h * HALF, (h + 1) * HALF)
                        if n == 0:
                            pe.wait_ge(x0_lo_made[h], 1)
                        nc.tensor.matmul(to[:, part], wqk_hi[:, w], x_lo[0][:, part], start=False,
                                         stop=True).then_inc(qk0_mm, 1)

            def project_qk(s):
                p, to, w = s % 2, ring_tile("QK", s, 0), slice(2 * P * layer(s), 2 * P * layer(s) + P)
                pe.wait_ge(x_cut, s)
                wait_for_ring(pe, "QK", s, 0)
                for n, (weight, x) in enumerate(((wqk_hi, x_hi[p]), (wqk_lo, x_hi[p]), (wqk_hi, x_lo[p]))):
                    for h in range(2):
                        part = slice(h * HALF, (h + 1) * HALF)
                        last = nc.tensor.matmul(to[:, part], weight[:, w], x[:, part], start=(n == 0),
                                                stop=(n == 2))
                last.then_inc(qk_mm, 1)

            def project_v(s):
                l, to = layer(s), ring_tile("V", s, 0)
                if s == 0:
                    pe.wait_ge(late_loaded, 16)
                    pe.wait_ge(x0_loaded[0], 16)
                    pe.wait_ge(x0_loaded[1], 16)
                elif s < B:
                    pe.wait_ge(x_loaded[s], 16)
                else:
                    pe.wait_ge(x_made, 2 * (s - B + 1))
                wait_for_ring(pe, "V", s, 0)
                for j in range(TILES):
                    last = nc.tensor.matmul(to[:, j * C:(j + 1) * C], x_all[:, s, j * P:(j + 1) * P], late[:, l, :],
                                            start=True, stop=True)
                last.then_inc(v_mm, 1)

            def energies(s, i):
                p, to, rows = s % 2, ring_tile("E", s, i), slice(i * P, (i + 1) * P)
                if s == 0 and i == 0:
                    pe.wait_ge(stacked0_made, 4)
                elif i == 0:
                    pe.wait_ge(swapped[s % 2], 32 * ((s + 1) // 2))
                wait_for_ring(pe, "E", s, i)
                nc.tensor.matmul(to[:, 0:HALF], qk[p][0:64, rows], qk_swapped[p][0:64, 0:HALF],
                                 start=True, stop=True)
                nc.tensor.matmul(to[:, HALF:N], qk_swapped[p][64:128, rows], qk[p][64:128, HALF:N],
                                 start=True, stop=True).then_inc(e_mm, 1)

            def transpose_shift(s):
                if s == 0:
                    pe.wait_ge(late_loaded, 16)
                wait_for_ring(pe, "shift", s, 0)
                pe.wait_ge(log_made, s + 1)
                pe.wait_ge(max_twice, s + 1)
                to = ring_tile("shift", s, 0)[0:2 * TILES, 0:P]
                nc.tensor.matmul(to, neg_max[s % 2][:], late[:, IDENTITY], start=True, stop=False)
                nc.tensor.matmul(to, log_sum[s % 2][:], late[:, IDENTITY + 1], start=False,
                                 stop=True).then_inc(shift_mm, 1)

            def energies_transposed(s, k):
                p, j, to = s % 2, ORDER[k], ring_tile("ET", s, k)
                rows = slice(j * P, (j + 1) * P)
                if k == 0:
                    pe.wait_ge(shift_placed, 32 * (s + 1))
                wait_for_ring(pe, "ET", s, k)
                nc.tensor.matmul(to[:, 0:HALF], k_twice[p][0:64, rows], q_shifted[p][0:64, 0:HALF],
                                 start=True, stop=True)
                nc.tensor.matmul(to[:, HALF:N], k_twice[p][64:128, rows],
                                 q_shifted[p][64:128, HALF:N], start=True, stop=True).then_inc(et_mm, 1)

            def times_v(s, k):
                p, j = s % 2, ORDER[k]
                if k == 0:
                    pe.wait_ge(v_made, s + 1)
                if j < NATIVE:
                    pe.wait_ge(attn_made, TILES * s + k + 1)
                    passes = ((v32[p][:, j], attn[:, j]),)
                else:
                    wait_for_hi(pe, s, k)
                    c = j - NATIVE
                    passes = ((v_hi[p][:, c], attn_hi[:, c]), (v_lo[p][:, c], attn_hi[:, c]),
                              (v_hi[p][:, c], attn_lo[:, c]))
                work = [(n, h) for n in range(len(passes)) for h in range(2)]
                if k == TILES - 1:
                    work.sort(key=lambda nh: nh[1])
                for n, h in work:
                    part = slice(h * HALF, (h + 1) * HALF)
                    if k == 0 and n == 0:
                        at_least(pe, x_made, 2 * (s - 1) + h + 1)
                    if n == 2 and h == 0:
                        wait_for_lo(pe, s, k)
                    v, a = passes[n]
                    last = nc.tensor.matmul(out_psum[:, part], v, a[:, part], start=(k == 0 and n == 0),
                                            stop=(k == TILES - 1 and n == len(passes) - 1))
                    if k == TILES - 1 and (n, h) == (len(passes) - 1, 0):
                        last.then_inc(pv_half_mm, 1)
                last.then_inc(pv_mm, 1)

            def keep_warm(count):
                for _n in range(count):
                    nc.tensor.matmul(out_psum[:, 0:HALF], zeros[:, 0:P], zeros[:], start=True, stop=True)

            pe.wait_ge(zeros_made, 1)
            keep_warm(WARM_UP)
            for n, (what, s, i) in enumerate(in_order(PE_FIRST, PE_STEP)):
                if n < len(KEEP_WARM):
                    keep_warm(KEEP_WARM[n])
                if what == "ET":
                    energies_transposed(s, i)
                elif what == "E":
                    energies(s, i)
                elif what == "PV":
                    times_v(s, i)
                elif what == "V":
                    project_v(s)
                elif what == "QK" and s > 0:
                    project_qk(s)
                elif what == "QK":
                    project_qk0()
                elif what == "QK swapped":
                    pass
                else:
                    transpose_shift(s)


def kernel(x, L0_conv_Wq, L0_conv_bq, L0_conv_Wk, L0_conv_bk, L0_conv_Wv, L0_conv_bv, L0_conv_gamma,
           L1_conv_wq, L1_conv_bq, L1_conv_wk, L1_conv_bk, L1_conv_wv, L1_conv_bv, L1_conv_gamma):
    import numpy as np
    import concourse.bacc as bacc
    from concourse.bass_utils import run_bass_kernel_spmd

    f32 = np.float32
    layers = [(L0_conv_Wq, L0_conv_bq, L0_conv_Wk, L0_conv_bk, L0_conv_Wv, L0_conv_bv, L0_conv_gamma),
              (L1_conv_wq, L1_conv_bq, L1_conv_wk, L1_conv_bk, L1_conv_wv, L1_conv_bv, L1_conv_gamma)]
    layers = [[np.asarray(a) for a in l] for l in layers]
    wqk = np.zeros((P, QK_SETS, P), f32)
    columns = np.zeros((P, COLUMNS), f32)
    late = np.zeros((P, LATE, P), f32)
    for n, l, q_at, k_at, bias in ((0, 0, 0, 64, 0), (1, 0, 64, 0, SWAPPED_BIAS), (2, 1, 0, 64, 1)):
        wq_l, bq_l, wk_l, bk_l = layers[l][:4]
        for copy in range(3):
            for w_l, b_l, at in ((wq_l, bq_l, q_at), (wk_l, bk_l, k_at)):
                rows = slice(at + copy * RD, at + (copy + 1) * RD)
                wqk[:, n, rows] = w_l.T
                columns[rows, bias] = b_l
        columns[k_at + SHIFT_ROW:k_at + SHIFT_ROW + 2, bias] = 1.0
    for l, (_wq, _bq, _wk, _bk, wv_l, bv_l, gamma_l) in enumerate(layers):
        columns[:, GAMMA + l] = gamma_l[0]
        late[:, l] = wv_l.T
        late[:, LAYERS + l] = bv_l[None, :]
    late[:, IDENTITY] = np.eye(P, dtype=f32)
    late[:, IDENTITY + 1] = -late[:, IDENTITY]
    for column, q_at, k_at in ((MASK, 0, 64), (SWAPPED_MASK, 64, 0)):
        columns[q_at + 2 * RD:q_at + 3 * RD, column] = 1.0
        columns[k_at + RD:k_at + 2 * RD, column] = 1.0
    columns[TILES:2 * TILES, SHIFT_MASK] = 1.0
    arrays = {
        "x_in": np.ascontiguousarray(np.asarray(x).reshape(B, C, N)),
        "weights_in": np.concatenate([wqk.reshape(P, QK_SETS * P), columns], axis=1),
        "late_in": late,
    }
    nc = bacc.Bacc("TRN2", target_bir_lowering=False, num_devices=1)
    fp32 = mybir.dt.float32
    args = [nc.dram_tensor(name, a.shape, fp32, kind="ExternalInput").ap() for name, a in arrays.items()]
    out = nc.dram_tensor("out_dram", (B, C, N), fp32, kind="ExternalOutput").ap()
    build_attention_layers(nc, *args, out)
    r = run_bass_kernel_spmd(nc, [arrays], core_ids=[0])
    return r.results[0]["out_dram"].reshape(B, C, 32, 32)
```
